# Optimizing a Trainium2 kernel written in Bass

```python
import numpy as np
import jax
import jax.numpy as jnp

def _softmax(x, axis=-1):
    return jax.nn.softmax(x, axis=axis)

def _gelu(x):
    return jax.nn.gelu(x, approximate=True)

def _silu(x):
    return jax.nn.silu(x)

def _sigmoid(x):
    return jax.nn.sigmoid(x)

def _layernorm(x, axis=-1, eps=1e-05):
    m = jnp.mean(x, axis=axis, keepdims=True)
    v = jnp.var(x, axis=axis, keepdims=True)
    return (x - m) / jnp.sqrt(v + eps)

def _scatter_add(tgt, idx, src, axis=0):
    return tgt.at[idx].add(src)

def _segment_sum(src, seg, n):
    return jax.ops.segment_sum(src, seg, n)
kernel_name = 'mk_dlrm_tower_d1_rec_r8_e66ad3'

def setup_inputs(seed: int=0):
    np.random.seed(seed)
    _w = jnp.asarray

    def _rec_inputs():
        import jax
        import jax.numpy as jnp
        _tk = jax.random.key(seed)
        ids = jnp.stack([jax.random.randint(jax.random.fold_in(_tk, 200 + f), (2048,), 0, v, jnp.int32) for f, v in enumerate([12500, 1250, 1250, 1250, 1000, 1000, 1250, 12500, 12500, 125000, 12500, 1000, 1250, 1000, 12500, 12500, 1000, 1250, 1000, 12500, 1000, 1250, 1000, 1000, 12500, 1250])], axis=1)
        tbl_0 = 0.05 * jax.random.normal(jax.random.fold_in(_tk, 500 + 0), (12500, 128), jnp.float32)
        tbl_1 = 0.05 * jax.random.normal(jax.random.fold_in(_tk, 500 + 1), (1250, 128), jnp.float32)
        tbl_2 = 0.05 * jax.random.normal(jax.random.fold_in(_tk, 500 + 2), (1250, 128), jnp.float32)
        tbl_3 = 0.05 * jax.random.normal(jax.random.fold_in(_tk, 500 + 3), (1250, 128), jnp.float32)
        tbl_4 = 0.05 * jax.random.normal(jax.random.fold_in(_tk, 500 + 4), (1000, 128), jnp.float32)
        tbl_5 = 0.05 * jax.random.normal(jax.random.fold_in(_tk, 500 + 5), (1000, 128), jnp.float32)
        tbl_6 = 0.05 * jax.random.normal(jax.random.fold_in(_tk, 500 + 6), (1250, 128), jnp.float32)
        tbl_7 = 0.05 * jax.random.normal(jax.random.fold_in(_tk, 500 + 7), (12500, 128), jnp.float32)
        tbl_8 = 0.05 * jax.random.normal(jax.random.fold_in(_tk, 500 + 8), (12500, 128), jnp.float32)
        tbl_9 = 0.05 * jax.random.normal(jax.random.fold_in(_tk, 500 + 9), (125000, 128), jnp.float32)
        tbl_10 = 0.05 * jax.random.normal(jax.random.fold_in(_tk, 500 + 10), (12500, 128), jnp.float32)
        tbl_11 = 0.05 * jax.random.normal(jax.random.fold_in(_tk, 500 + 11), (1000, 128), jnp.float32)
        tbl_12 = 0.05 * jax.random.normal(jax.random.fold_in(_tk, 500 + 12), (1250, 128), jnp.float32)
        tbl_13 = 0.05 * jax.random.normal(jax.random.fold_in(_tk, 500 + 13), (1000, 128), jnp.float32)
        tbl_14 = 0.05 * jax.random.normal(jax.random.fold_in(_tk, 500 + 14), (12500, 128), jnp.float32)
        tbl_15 = 0.05 * jax.random.normal(jax.random.fold_in(_tk, 500 + 15), (12500, 128), jnp.float32)
        tbl_16 = 0.05 * jax.random.normal(jax.random.fold_in(_tk, 500 + 16), (1000, 128), jnp.float32)
        tbl_17 = 0.05 * jax.random.normal(jax.random.fold_in(_tk, 500 + 17), (1250, 128), jnp.float32)
        tbl_18 = 0.05 * jax.random.normal(jax.random.fold_in(_tk, 500 + 18), (1000, 128), jnp.float32)
        tbl_19 = 0.05 * jax.random.normal(jax.random.fold_in(_tk, 500 + 19), (12500, 128), jnp.float32)
        tbl_20 = 0.05 * jax.random.normal(jax.random.fold_in(_tk, 500 + 20), (1000, 128), jnp.float32)
        tbl_21 = 0.05 * jax.random.normal(jax.random.fold_in(_tk, 500 + 21), (1250, 128), jnp.float32)
        tbl_22 = 0.05 * jax.random.normal(jax.random.fold_in(_tk, 500 + 22), (1000, 128), jnp.float32)
        tbl_23 = 0.05 * jax.random.normal(jax.random.fold_in(_tk, 500 + 23), (1000, 128), jnp.float32)
        tbl_24 = 0.05 * jax.random.normal(jax.random.fold_in(_tk, 500 + 24), (12500, 128), jnp.float32)
        tbl_25 = 0.05 * jax.random.normal(jax.random.fold_in(_tk, 500 + 25), (1250, 128), jnp.float32)
        _rk = jax.random.fold_in(_tk, 7)
        r_dense_features = -0.000520686 + 1.00062 * jax.random.normal(jax.random.fold_in(_rk, 101), (2048, 128), jnp.float32)
        W_top1 = 0.0405887 * jax.random.normal(jax.random.fold_in(_tk, 801), (607, 512), jnp.float32)
        W_top2 = 0.0441942 * jax.random.normal(jax.random.fold_in(_tk, 802), (512, 256), jnp.float32)
        W_top3 = 0.0625 * jax.random.normal(jax.random.fold_in(_tk, 803), (256, 1), jnp.float32)
        b_top1 = jnp.zeros((512,), jnp.float32)
        b_top2 = jnp.zeros((256,), jnp.float32)
        return (r_dense_features, ids, tbl_0, tbl_1, tbl_2, tbl_3, tbl_4, tbl_5, tbl_6, tbl_7, tbl_8, tbl_9, tbl_10, tbl_11, tbl_12, tbl_13, tbl_14, tbl_15, tbl_16, tbl_17, tbl_18, tbl_19, tbl_20, tbl_21, tbl_22, tbl_23, tbl_24, tbl_25, W_top1, b_top1, W_top2, b_top2, W_top3)
    r_dense_features, ids, tbl_0, tbl_1, tbl_2, tbl_3, tbl_4, tbl_5, tbl_6, tbl_7, tbl_8, tbl_9, tbl_10, tbl_11, tbl_12, tbl_13, tbl_14, tbl_15, tbl_16, tbl_17, tbl_18, tbl_19, tbl_20, tbl_21, tbl_22, tbl_23, tbl_24, tbl_25, W_top1, b_top1, W_top2, b_top2, W_top3 = _rec_inputs()

    def _L0_rec_setup():
        import jax, jax.numpy as jnp
        import numpy as np
        F = 26
        B, D = (2048, 128)
        _IU0, _IU1 = np.triu_indices(F + 1, k=1)
        _IU0 = jnp.asarray(_IU0)
        _IU1 = jnp.asarray(_IU1)
        key = jax.random.key(seed)
        k1, k2 = jax.random.split(key)
        dense_features = jax.random.normal(k1, (B, D), dtype=jnp.float32)
        sparse_features = jax.random.normal(k2, (B, F, D), dtype=jnp.float32)
        return {'dense_features': dense_features, 'sparse_features': sparse_features}
    _L0_rec_all = _L0_rec_setup()
    _L0_rec_in = {k: v for k, v in _L0_rec_all.items() if k in ()}
    del _L0_rec_all
    return {'r_dense_features': r_dense_features, 'ids': ids, 'tbl_0': tbl_0, 'tbl_1': tbl_1, 'tbl_2': tbl_2, 'tbl_3': tbl_3, 'tbl_4': tbl_4, 'tbl_5': tbl_5, 'tbl_6': tbl_6, 'tbl_7': tbl_7, 'tbl_8': tbl_8, 'tbl_9': tbl_9, 'tbl_10': tbl_10, 'tbl_11': tbl_11, 'tbl_12': tbl_12, 'tbl_13': tbl_13, 'tbl_14': tbl_14, 'tbl_15': tbl_15, 'tbl_16': tbl_16, 'tbl_17': tbl_17, 'tbl_18': tbl_18, 'tbl_19': tbl_19, 'tbl_20': tbl_20, 'tbl_21': tbl_21, 'tbl_22': tbl_22, 'tbl_23': tbl_23, 'tbl_24': tbl_24, 'tbl_25': tbl_25, 'W_top1': W_top1, 'b_top1': b_top1, 'W_top2': W_top2, 'b_top2': b_top2, 'W_top3': W_top3}

def reference(r_dense_features, ids, tbl_0, tbl_1, tbl_2, tbl_3, tbl_4, tbl_5, tbl_6, tbl_7, tbl_8, tbl_9, tbl_10, tbl_11, tbl_12, tbl_13, tbl_14, tbl_15, tbl_16, tbl_17, tbl_18, tbl_19, tbl_20, tbl_21, tbl_22, tbl_23, tbl_24, tbl_25, W_top1, b_top1, W_top2, b_top2, W_top3):
    import jax
    import jax.numpy as jnp

    def _L0_rec_ref(dense_features, sparse_features):
        import jax, jax.numpy as jnp
        import numpy as np
        F = 26
        B, D = (2048, 128)
        _IU0, _IU1 = np.triu_indices(F + 1, k=1)
        _IU0 = jnp.asarray(_IU0)
        _IU1 = jnp.asarray(_IU1)
        combined = jnp.concatenate([dense_features[:, None, :], sparse_features], axis=1)
        interactions = jnp.einsum('bfd,bgd->bfg', combined, combined)
        interactions_flat = interactions[:, _IU0, _IU1]
        return jnp.concatenate([dense_features, interactions_flat], axis=1)
    e = jnp.stack([tbl_0[ids[:, 0]], tbl_1[ids[:, 1]], tbl_2[ids[:, 2]], tbl_3[ids[:, 3]], tbl_4[ids[:, 4]], tbl_5[ids[:, 5]], tbl_6[ids[:, 6]], tbl_7[ids[:, 7]], tbl_8[ids[:, 8]], tbl_9[ids[:, 9]], tbl_10[ids[:, 10]], tbl_11[ids[:, 11]], tbl_12[ids[:, 12]], tbl_13[ids[:, 13]], tbl_14[ids[:, 14]], tbl_15[ids[:, 15]], tbl_16[ids[:, 16]], tbl_17[ids[:, 17]], tbl_18[ids[:, 18]], tbl_19[ids[:, 19]], tbl_20[ids[:, 20]], tbl_21[ids[:, 21]], tbl_22[ids[:, 22]], tbl_23[ids[:, 23]], tbl_24[ids[:, 24]], tbl_25[ids[:, 25]]], axis=1)
    z = _L0_rec_ref(r_dense_features, e)
    z = z.reshape(z.shape[0], -1)
    h = jnp.concatenate([z, r_dense_features], axis=1)
    h = jnp.maximum(h @ W_top1 + b_top1, 0.0)
    h = jnp.maximum(h @ W_top2 + b_top2, 0.0)
    y = h @ W_top3
    return y

_drawn_inputs = setup_inputs


def setup_inputs(seed=0):
    import zlib

    import numpy as np

    out = dict(_drawn_inputs(seed))
    spreads = {'b_top1': (0.0, 0.1), 'b_top2': (0.0, 0.1)}
    factors = {}
    for name, (base, spread) in spreads.items():
        noise = np.random.default_rng([zlib.crc32(name.encode()), seed]).standard_normal(out[name].shape)
        drawn = base * np.exp(spread * noise) if base else spread * noise
        out[name] = jnp.asarray(drawn.astype(out[name].dtype))
    for name, factor in factors.items():
        out[name] = (out[name] * factor).astype(out[name].dtype)
    return out
```

```python
from contextlib import ExitStack

import concourse.bass as bass
from concourse import mybir

F32 = mybir.dt.float32
I32 = mybir.dt.int32
U32 = mybir.dt.uint32
ALU = mybir.AluOpType
ACT = mybir.ActivationFunctionType

B, D, F = 2048, 128, 26
C = F + 1
T = 128
PAIR = 2 * T
NP = B // PAIR
N1, N2 = 512, 256
QUAD = 4
NQ = -(-F // QUAD)
SLOT = 32
GS = T // 4
GB = 4
NG = GS // GB
MG = 3 * SLOT + C
BLK = 4 * C
HALF = C // 2
RPC = 9
KP = RPC * HALF
NCH = C * HALF // KP
M1, M2 = N1 // 128, N2 // 128


def pair_rows():
    rows = [(C + 1) * p + k for p in range(C - 1) for k in range(1, HALF + 1)]
    return rows + [(C + 1) * p + HALF + 1 for p in range(HALF)]


def program(nc, x_t, ids, tables, w_dense, w_pairs, b1, w2, b2, w3, out):
    ctx = ExitStack()
    with ctx:
        def sb(name, shape, dt=F32):
            return ctx.enter_context(nc.sbuf_tensor(name, shape, dt))

        def ps(name, shape):
            return ctx.enter_context(nc.psum_tensor(name, shape, F32))

        def sem(name):
            return ctx.enter_context(nc.semaphore(name))

        square = nc.dram_tensor("square", (C * C, PAIR), F32, kind="Internal").ap()

        ident = sb("ident", [128, 128])
        index = [sb(f"index{a}", [T, F], I32) for a in range(2)]
        rows = [sb(f"rows{a}", [T, F, D]) for a in range(2)]
        feats = [sb(f"feats{a}", [D, GS, 4, SLOT]) for a in range(2)]
        prods = [sb(f"prods{a}", [MG, BLK, GS]) for a in range(2)]
        pairs = sb("pairs", [KP, NCH, PAIR])
        dense = sb("dense", [D, B])
        h1 = sb("h1", [128, M1, PAIR])
        h2 = sb("h2", [128, M2, PAIR])
        wd = sb("wd", [D, 2, N1])
        wdense = sb("wdense", [D, N1])
        wpairs = sb("wpairs", [KP, NCH, N1])
        w2s = sb("w2s", [128, M1, N2])
        w3s = sb("w3s", [128, M2])
        b1s = sb("b1s", [128, M1])
        b2s = sb("b2s", [128, M2])
        y = sb("y", [1, B])

        p_tr = [ps(f"p_tr{k}", [128, QUAD, T]) for k in range(2)]
        p_gr = [ps(f"p_gr{k}", [128, 512]) for k in range(2)]
        p_mlp = [ps(f"p_mlp{k}", [128, 512]) for k in range(2)]

        s_ident = sem("s_ident")
        s_pad = sem("s_pad")
        s_dense = sem("s_dense")
        s_weights = sem("s_weights")
        s_wdense = sem("s_wdense")
        s_index = [sem(f"s_index{a}") for a in range(2)]
        s_rows = [[sem(f"s_rows{a}_{q}") for q in range(NQ)] for a in range(2)]
        s_turned = sem("s_turned")
        s_feats = sem("s_feats")
        s_fdense = sem("s_fdense")
        s_gram = sem("s_gram")
        s_prods = sem("s_prods")
        s_stored = [sem(f"s_stored{a}") for a in range(2)]
        s_pairs = sem("s_pairs")
        s_h1 = sem("s_h1")
        s_h1r = sem("s_h1r")
        s_h2 = sem("s_h2")
        s_h2r = sem("s_h2r")
        s_y = sem("s_y")
        s_yr = sem("s_yr")
        s_out = sem("s_out")
        s_passed = sem("s_passed")

        def quad(q):
            return range(QUAD * q, min(QUAD * q + QUAD, F))

        block = ctx.enter_context(nc.Block())

        @block.sync
        def _(sp):
            for a in range(2):
                sp.dma_start(index[a][:, :], ids[a * T:a * T + T, :]).then_inc(s_index[a], 16)
            sp.dma_start(dense[:, :], x_t).then_inc(s_dense, 16)
            sp.dma_start(wd[:, :, :], w_dense.rearrange("a d n -> d a n")).then_inc(s_weights, 16)
            sp.dma_start(wpairs[:, :, :], w_pairs.rearrange("c p n -> p c n")).then_inc(s_weights, 16)
            sp.dma_start(w2s[:, :, :], w2.rearrange("(k p) n -> p k n", p=128)).then_inc(s_weights, 16)
            sp.dma_start(w3s[:, :], w3).then_inc(s_weights, 16)
            sp.dma_start(b1s[:, :], b1).then_inc(s_weights, 16)
            sp.dma_start(b2s[:, :], b2).then_inc(s_weights, 16)

            def pair(i, first=False, last=False):
                for a in range(2):
                    if not last:
                        sp.wait_ge(s_turned, (2 * i + a + 1) * NQ)
                        sp.sem_inc(s_passed, 1)
                        sp.dma_start(index[a][:, :], ids[bass.ds((2 * i + 2 + a) * T, T), :])\
                          .then_inc(s_index[a], 16)
                    sp.wait_ge(s_prods, (2 * i + a + 1) * NG)
                    sp.sem_inc(s_passed, 1)
                    if not first and a == 0:
                        sp.wait_ge(s_pairs, 64 * i)
                    for j in range(4):
                        dst = square.rearrange("(f g) s -> f g s", g=C)
                        lo = a * T + j * GS
                        sp.dma_start(dst[:, :, lo:lo + GS],
                                     prods[a][SLOT * j:SLOT * j + C, C * j:C * j + C, :])\
                          .then_inc(s_stored[a], 16)
                for a in range(2):
                    sp.wait_ge(s_stored[a], 64 * i + 64)
                    sp.sem_inc(s_passed, 1)
                if not first:
                    sp.wait_ge(s_h1, M1 * i)
                for c in range(NCH):
                    n = min(RPC, C - 1 - c * RPC)
                    src = bass.AP(square.tensor, ((C + 1) * RPC * c + 1) * PAIR,
                                  [[(C + 1) * PAIR, n], [PAIR, HALF], [1, PAIR]])
                    sp.dma_start(pairs[0:n * HALF, c, :], src).then_inc(s_pairs, 16)
                src = bass.AP(square.tensor, (HALF + 1) * PAIR, [[(C + 1) * PAIR, HALF], [1, PAIR]])
                sp.dma_start(pairs[KP - HALF:KP, NCH - 1, :], src).then_inc(s_pairs, 16)

            pair(0, first=True)
            with sp.Fori(1, NP - 1) as i:
                pair(i)
            pair(NP - 1, last=True)
            sp.wait_ge(s_yr, NP)
            sp.dma_start(out, y[:, :]).then_inc(s_out, 16)
            sp.wait_ge(s_out, 16)

        @block.gpsimd
        def _(pool):
            pool.wait_ge(s_pad, 1)
            pool.affine_select(out=ident[:, :], in_=ident[:, :], compare_op=ALU.not_equal, fill=1.0,
                               base=0, pattern=[[-1, 128]], channel_multiplier=1).then_inc(s_ident, 1)

            def pair(i, first=False):
                for a in range(2):
                    pool.wait_ge(s_index[a], 16 * (i + 1))
                    for q in range(NQ):
                        if not first:
                            pool.wait_ge(s_turned, (2 * i + a - 2) * NQ + q + 1)
                            pool.sem_inc(s_passed, 1)
                        for f in quad(q):
                            pool.indirect_dma_start(
                                out=rows[a][:, f, :], out_offset=None, in_=tables[f],
                                in_offset=bass.IndirectOffsetOnAxis(
                                    ap=index[a][:, f:f + 1].bitcast(U32), axis=0),
                            ).then_inc(s_rows[a][q], 16)

            pair(0, first=True)
            with pool.Fori(1, NP) as i:
                pair(i)

        @block.tensor
        def _(pe):
            pe.wait_ge(s_ident, 1)
            pe.wait_ge(s_pad, 3)

            def turn(i, a, q):
                n = NQ * (2 * i + a) + q
                pe.wait_ge(s_rows[a][q], 16 * len(quad(q)) * (i + 1))
                if not (isinstance(n, int) and n < 2):
                    pe.wait_ge(s_feats, n - 1)
                for k, f in enumerate(quad(q)):
                    mm = pe.transpose(p_tr[(NQ * a + q) % 2][:, k, :], rows[a][:, f, :], ident[:, :])
                mm.then_inc(s_turned, 1)

            def gram(i, a):
                t = 2 * i + a
                pe.wait_ge(s_feats, NQ * (t + 1))
                pe.wait_ge(s_fdense, t + 1)
                for b in range(NG):
                    n = NG * t + b
                    if not (isinstance(n, int) and n < 2):
                        pe.wait_ge(s_prods, n - 1)
                    for k in range(GB):
                        group = feats[a][:, GB * b + k, :, :]
                        mm = pe.matmul(p_gr[b % 2][0:MG, BLK * k:BLK * k + BLK],
                                       group.rearrange("d j f -> d (j f)")[:, 0:MG], group[:, :, 0:C],
                                       start=True, stop=True)
                    mm.then_inc(s_gram, 1)

            def mlp(i, first=False):
                for m in range(M1):
                    if m >= 2:
                        pe.wait_ge(s_h1r, M1 * i + m - 1)
                    elif m == 0 and not first:
                        pe.wait_ge(s_yr, i)
                    cols = slice(128 * m, 128 * m + 128)
                    o = p_mlp[m % 2][:, 0:PAIR]
                    pe.matmul(o, wdense[:, cols], dense[:, bass.ds(i * PAIR, PAIR)], start=True, stop=False)
                    if m == 0:
                        pe.wait_ge(s_pairs, 64 * (i + 1))
                    for c in range(NCH):
                        mm = pe.matmul(o, wpairs[:, c, cols], pairs[:, c, :], start=False,
                                       stop=(c == NCH - 1))
                    mm.then_inc(s_h1, 1)
                pe.wait_ge(s_h1r, M1 * (i + 1))
                for m in range(M2):
                    for k in range(M1):
                        mm = pe.matmul(p_mlp[m % 2][:, 0:PAIR], w2s[:, k, 128 * m:128 * m + 128], h1[:, k, :],
                                       start=(k == 0), stop=(k == M1 - 1))
                    mm.then_inc(s_h2, 1)
                pe.wait_ge(s_h2r, M2 * (i + 1))
                for k in range(M2):
                    mm = pe.matmul(p_mlp[0][0:1, 0:PAIR], w3s[:, k:k + 1], h2[:, k, :], start=(k == 0),
                                   stop=(k == M2 - 1))
                mm.then_inc(s_y, 1)

            def pair(i, first=False, mlp_first=False):
                for q in range(NQ):
                    turn(i, 0, q)
                    if q == 2 and not first:
                        mlp(i - 1, first=mlp_first)
                gram(i, 0)
                for q in range(NQ):
                    turn(i, 1, q)
                gram(i, 1)

            pair(0, first=True)
            pe.wait_ge(s_weights, 96)
            pe.wait_ge(s_wdense, 1)
            pe.wait_ge(s_dense, 16)
            pair(1, mlp_first=True)
            with pe.Fori(2, NP) as i:
                pair(i)
            mlp(NP - 1)

        @block.scalar
        def _(act):
            def keep(i, a, q):
                n = NQ * (2 * i + a) + q
                act.wait_ge(s_turned, n + 1)
                k = len(quad(q))
                dst = feats[a][:, :, :, 1 + QUAD * q:1 + QUAD * q + k].rearrange("d g j f -> d f j g")
                src = p_tr[(NQ * a + q) % 2][:, 0:k, :].rearrange("d f (j g) -> d f j g", j=4)
                nc.scalar.activation(dst, src, ACT.Copy).then_inc(s_feats, 1)

            def keep_dense(i, a):
                src = dense[:, bass.ds((2 * i + a) * T, T)].rearrange("d (j g) -> d j g", j=4)
                nc.scalar.activation(feats[a][:, :, :, 0].rearrange("d g j -> d j g"), src,
                                     ACT.Copy).then_inc(s_fdense, 1)

            def mlp(i):
                for m in range(M1):
                    act.wait_ge(s_h1, M1 * i + m + 1)
                    nc.scalar.activation(h1[:, m, :], p_mlp[m % 2][:, 0:PAIR], ACT.Relu,
                                         bias=b1s[:, m:m + 1]).then_inc(s_h1r, 1)
                for m in range(M2):
                    act.wait_ge(s_h2, M2 * i + m + 1)
                    nc.scalar.activation(h2[:, m, :], p_mlp[m % 2][:, 0:PAIR], ACT.Relu,
                                         bias=b2s[:, m:m + 1]).then_inc(s_h2r, 1)
                act.wait_ge(s_y, i + 1)
                nc.scalar.activation(y[:, bass.ds(i * PAIR, PAIR)], p_mlp[0][0:1, 0:PAIR], ACT.Copy).then_inc(s_yr, 1)

            def pair(i, first=False):
                for a in range(2):
                    if not first:
                        act.wait_ge(s_gram, NG * (2 * i + a - 1))
                    keep_dense(i, a)
                    for q in range(NQ):
                        keep(i, a, q)
                        if a == 0 and q == 2 and not first:
                            mlp(i - 1)

            act.wait_ge(s_dense, 16)
            pair(0, first=True)
            act.wait_ge(s_weights, 96)
            with act.Fori(1, NP) as i:
                pair(i)
            mlp(NP - 1)

        @block.vector
        def _(dve):
            nc.vector.memset(ident[:, :], 0.0).then_inc(s_pad, 1)
            for a in range(2):
                nc.vector.memset(feats[a][:, :, :, C:], 0.0).then_inc(s_pad, 1)
            dve.wait_ge(s_weights, 96)
            nc.vector.tensor_tensor(wdense[:, :], wd[:, 0, :], wd[:, 1, :], ALU.add).then_inc(s_wdense, 1)

            def pair(i, first=False):
                for a in range(2):
                    t = 2 * i + a
                    if not first:
                        dve.wait_ge(s_stored[a], 64 * i)
                    for b in range(NG):
                        dve.wait_ge(s_gram, NG * t + b + 1)
                        src = p_gr[b % 2][0:MG, 0:GB * BLK].rearrange("p (g c) -> p c g", g=GB)
                        nc.vector.tensor_copy(prods[a][:, :, GB * b:GB * b + GB], src).then_inc(s_prods, 1)

            pair(0, first=True)
            with dve.Fori(1, NP) as i:
                pair(i)


def kernel(**inputs):
    import numpy as np
    import concourse.bacc as bacc
    from concourse.bass_utils import run_bass_kernel_spmd

    w1 = np.asarray(inputs["W_top1"])
    f, g = np.triu_indices(C, k=1)
    row_of = {(int(p), int(q)): D + n for n, (p, q) in enumerate(zip(f, g))}
    order = [row_of[tuple(sorted(divmod(r, C)))] for r in pair_rows()]
    arrays = {
        "in_x_t": np.ascontiguousarray(np.asarray(inputs["r_dense_features"]).T),
        "in_ids": np.ascontiguousarray(inputs["ids"]),
        "in_w_dense": np.ascontiguousarray(np.stack([w1[0:D], w1[D + len(f):]])),
        "in_w_pairs": np.ascontiguousarray(w1[order].reshape(NCH, KP, N1)),
        "in_b1": np.ascontiguousarray(np.asarray(inputs["b_top1"]).reshape(M1, 128).T),
        "in_w2": np.ascontiguousarray(inputs["W_top2"]),
        "in_b2": np.ascontiguousarray(np.asarray(inputs["b_top2"]).reshape(M2, 128).T),
        "in_w3": np.ascontiguousarray(np.asarray(inputs["W_top3"]).reshape(M2, 128).T),
    }
    for n in range(F):
        arrays[f"in_table_{n}"] = np.ascontiguousarray(inputs[f"tbl_{n}"])
    nc = bacc.Bacc("TRN2", target_bir_lowering=False, num_devices=1)
    ap = {k: nc.dram_tensor(k, a.shape, mybir.dt.from_np(a.dtype), kind="ExternalInput").ap()
          for k, a in arrays.items()}
    out = nc.dram_tensor("out_y", (B, 1), F32, kind="ExternalOutput").ap()
    program(nc, ap["in_x_t"], ap["in_ids"], [ap[f"in_table_{n}"] for n in range(F)], ap["in_w_dense"],
            ap["in_w_pairs"], ap["in_b1"], ap["in_w2"], ap["in_b2"], ap["in_w3"],
            out.rearrange("s a -> a s"))
    r = run_bass_kernel_spmd(nc, [arrays], core_ids=[0])
    return r.results[0]["out_y"]
```

```python
from contextlib import ExitStack

import concourse.bass as bass
from concourse import mybir

F32 = mybir.dt.float32
I32 = mybir.dt.int32
U32 = mybir.dt.uint32
F32R = mybir.dt.float32r
ALU = mybir.AluOpType
ACT = mybir.ActivationFunctionType

B, D, F = 2048, 128, 26
C = F + 1
T = 128
PAIR = 2 * T
NP = B // PAIR
N1, N2 = 512, 256
QUAD = 4
GS = T // 4
BLK = 4 * C
GB = 4
NG = GS // GB
HALF = C // 2
RPC = 9
KP = RPC * HALF
NCH = C * HALF // KP
M1, M2 = N1 // 128, N2 // 128

SEL_FIRST, SEL = 8, 6
VS = 1000
VC = -(-VS // 128)
VR = VS - 128 * (VC - 1)
STAGES = BLK * GS // (VC * D)
RING = 3
NGATHER = F - SEL
HIGH = -(1 << 12)


def feature_order(sizes):
    last = [n for n in range(F) if sizes[n] == VS][-SEL_FIRST:]
    return [n for n in range(F) if n not in last] + last


def pair_rows():
    rows = [(C + 1) * p + k for p in range(C - 1) for k in range(1, HALF + 1)]
    return rows + [(C + 1) * p + HALF + 1 for p in range(HALF)]


PIECES = ((slice(0, 128), slice(0, VC - 1)), (slice(0, VR), slice(VC - 1, VC)))


def selected(first):
    return SEL_FIRST if first else SEL


def quads(first):
    n = F - selected(first)
    return [range(k, min(k + QUAD, n)) for k in range(0, n, QUAD)]


NQ0, NQ = len(quads(True)), len(quads(False))


def quads_before(i, a):
    if isinstance(i, int) and i == 0:
        return NQ0 * a
    return (2 * i + a) * NQ + 2 * (NQ0 - NQ)


def selected_before(i):
    if isinstance(i, int) and i == 0:
        return 0
    return i * SEL + SEL_FIRST - SEL


def program(nc, x_t, ids, ids_t, tables, w_dense, w_pairs, b1, w2, b2, w3, out):
    ctx = ExitStack()
    with ctx:
        def sb(name, shape, dt=F32):
            return ctx.enter_context(nc.sbuf_tensor(name, shape, dt))

        def ps(name):
            return ctx.enter_context(nc.psum_tensor(name, [128, 512], F32))

        def sem(name):
            return ctx.enter_context(nc.semaphore(name))

        square = nc.dram_tensor("square", (C * C, PAIR), F32, kind="Internal").ap()

        ident = sb("ident", [128, 128])
        index = [sb(f"index{a}", [T, F], I32) for a in range(2)]
        rows = [sb(f"rows{a}", [T, NGATHER, D]) for a in range(2)]
        feats = [sb(f"feats{a}", [D, GS, 4, C]) for a in range(2)]
        prods = [sb(f"prods{a}", [128, BLK, GS]) for a in range(2)]
        piece = [prods[n].rearrange("p c g -> p (c g)")[:, k * VC * D:(k + 1) * VC * D]
                 .rearrange("p (c d) -> p c d", c=VC) for n in range(2) for k in range(STAGES)]
        raw, masked = piece[:STAGES], piece[STAGES:]
        pairs = sb("pairs", [KP, NCH, PAIR])
        ids_all = sb("ids_all", [128, SEL_FIRST, PAIR], I32)
        row_of = sb("row_of", [128, VC], I32)
        onehot = [sb(f"onehot{k}", [128, VC, PAIR], F32R) for k in range(RING)]
        high = [sb(f"high{k}", [128, VC, D], F32R) for k in range(SEL_FIRST)]
        low = [sb(f"low{k}", [128, VC, D], F32R) for k in range(SEL_FIRST)]
        dense = sb("dense", [D, B])
        h1 = sb("h1", [128, M1, PAIR])
        h2 = sb("h2", [128, M2, PAIR])
        wdense = sb("wdense", [D, 2, N1])
        wpairs = sb("wpairs", [KP, NCH, N1])
        w2s = sb("w2s", [128, M1, N2])
        w3s = sb("w3s", [128, M2])
        b1s = sb("b1s", [128, M1])
        b2s = sb("b2s", [128, M2])
        y = sb("y", [1, PAIR])

        p_turn = [ps(f"p_turn{k}") for k in range(2)]
        p_gram = [ps(f"p_gram{k}") for k in range(2)]
        p_sel = [ps(f"p_sel{k}") for k in range(2)]
        p_mlp = [ps(f"p_mlp{k}") for k in range(2)]

        s_zero = sem("s_zero")
        s_ident = sem("s_ident")
        s_row_of = sem("s_row_of")
        s_dense = sem("s_dense")
        s_weights = sem("s_weights")
        s_wdense = sem("s_wdense")
        s_table = [sem(f"s_table{k}") for k in range(SEL_FIRST)]
        s_masked = sem("s_masked")
        s_high = sem("s_high")
        s_low = sem("s_low")
        s_index = [sem(f"s_index{a}") for a in range(2)]
        s_rows = [[sem(f"s_rows{a}_{q}") for q in range(max(NQ, NQ0))] for a in range(2)]
        s_turned = sem("s_turned")
        s_feats = sem("s_feats")
        s_fdense = sem("s_fdense")
        s_ids_all = sem("s_ids_all")
        s_onehot = sem("s_onehot")
        s_sel = sem("s_sel")
        s_fsel = sem("s_fsel")
        s_gram = sem("s_gram")
        s_prods = sem("s_prods")
        s_stored = [sem(f"s_stored{a}") for a in range(2)]
        s_pairs = sem("s_pairs")
        s_h1 = sem("s_h1")
        s_h1r = sem("s_h1r")
        s_h2 = sem("s_h2")
        s_h2r = sem("s_h2r")
        s_y = sem("s_y")
        s_yr = sem("s_yr")
        s_out = sem("s_out")
        s_passed = sem("s_passed")

        block = ctx.enter_context(nc.Block())

        @block.sync
        def _(sp):
            def load_index(i, a):
                sp.dma_start(index[a][:, :], ids[bass.ds((2 * i + a) * T, T), :]).then_inc(s_index[a], 16)

            def load_ids_all(i, first=False):
                n = selected(first)
                src = ids_t[F - n:F, bass.ds(i * PAIR, PAIR)]
                src = src.rearrange("(o f) s -> o f s", o=1).to_broadcast([128, n, PAIR])
                sp.dma_start(ids_all[:, SEL_FIRST - n:SEL_FIRST, :], src).then_inc(s_ids_all, 16)

            for a in range(2):
                load_index(0, a)
            load_ids_all(0, first=True)
            for k in range(SEL_FIRST):
                t = tables[F - SEL_FIRST + k]
                whole = 128 * (VC - 1)
                if k >= STAGES:
                    sp.wait_ge(s_low, 2 * (k - STAGES + 1))
                sp.dma_start(raw[k % STAGES][:, 0:VC - 1, :], t[0:whole, :].rearrange("(c p) d -> p c d", p=128))\
                  .then_inc(s_table[k], 16)
                sp.dma_start(raw[k % STAGES][0:VR, VC - 1, :], t[whole:VS, :]).then_inc(s_table[k], 16)
                if k == 0:
                    sp.dma_start(dense[:, :], x_t).then_inc(s_dense, 16)
                if k == STAGES - 1:
                    sp.dma_start(wdense[:, :, :], w_dense.rearrange("a d n -> d a n")).then_inc(s_weights, 16)
                    sp.dma_start(wpairs[:, :, :], w_pairs.rearrange("c p n -> p c n")).then_inc(s_weights, 16)
                    sp.dma_start(w2s[:, :, :], w2.rearrange("(k p) n -> p k n", p=128)).then_inc(s_weights, 16)
                    sp.dma_start(w3s[:, :], w3).then_inc(s_weights, 16)
                    sp.dma_start(b1s[:, :], b1).then_inc(s_weights, 16)
                    sp.dma_start(b2s[:, :], b2).then_inc(s_weights, 16)

            def store(i, a, first=False):
                sp.wait_ge(s_prods, (2 * i + a + 1) * NG)
                sp.sem_inc(s_passed, 1)
                if a == 0 and not first:
                    sp.wait_ge(s_pairs, 64 * i)
                for j in range(4):
                    dst = square.rearrange("(f g) s -> f g s", g=C)
                    lo = a * T + j * GS
                    own = slice(C * j, C * j + C)
                    sp.dma_start(dst[:, :, lo:lo + GS], prods[a][own, own, :]).then_inc(s_stored[a], 16)

            def read_back(i, first=False):
                for a in range(2):
                    sp.wait_ge(s_stored[a], 64 * i + 64)
                    sp.sem_inc(s_passed, 1)
                if not first:
                    sp.wait_ge(s_h1, M1 * i)
                for c in range(NCH):
                    n = min(RPC, C - 1 - c * RPC)
                    src = bass.AP(square.tensor, ((C + 1) * RPC * c + 1) * PAIR,
                                  [[(C + 1) * PAIR, n], [PAIR, HALF], [1, PAIR]])
                    sp.dma_start(pairs[0:n * HALF, c, :], src).then_inc(s_pairs, 16)
                src = bass.AP(square.tensor, (HALF + 1) * PAIR, [[(C + 1) * PAIR, HALF], [1, PAIR]])
                sp.dma_start(pairs[KP - HALF:KP, NCH - 1, :], src).then_inc(s_pairs, 16)

            def result(i):
                sp.wait_ge(s_yr, i + 1)
                sp.sem_inc(s_passed, 1)
                sp.dma_start(out[:, bass.ds(i * PAIR, PAIR)], y[:, :]).then_inc(s_out, 16)

            def pair(i, first=False, second=False, last=False):
                if not first:
                    store(i - 1, 1, first=second)
                    read_back(i - 1, first=second)
                if not last:
                    sp.wait_ge(s_turned, quads_before(i, 1))
                    sp.sem_inc(s_passed, 1)
                    load_index(i + 1, 0)
                    sp.wait_ge(s_onehot, selected_before(i + 1))
                    sp.sem_inc(s_passed, 1)
                    load_ids_all(i + 1)
                store(i, 0, first=first)
                if not last:
                    sp.wait_ge(s_turned, quads_before(i + 1, 0))
                    sp.sem_inc(s_passed, 1)
                    load_index(i + 1, 1)
                if not first:
                    result(i - 1)

            pair(0, first=True)
            pair(1, second=True)
            with sp.Fori(2, NP - 1) as i:
                pair(i)
            pair(NP - 1, last=True)
            store(NP - 1, 1)
            read_back(NP - 1)
            result(NP - 1)
            sp.wait_ge(s_out, 16 * NP)

        @block.gpsimd
        def _(pool):
            def pair(i, first=False):
                for a in range(2):
                    pool.wait_ge(s_index[a], 16 * (i + 1))
                    pool.sem_inc(s_passed, 1)
                    for q, quad in enumerate(quads(first)):
                        if not first:
                            n = min(q + 1, NQ0) if isinstance(i, int) and i == 1 else q + 1
                            pool.wait_ge(s_turned, quads_before(i - 1, a) + n)
                            pool.sem_inc(s_passed, 1)
                        for f in quad:
                            pool.indirect_dma_start(
                                out=rows[a][:, f, :], out_offset=None, in_=tables[f],
                                in_offset=bass.IndirectOffsetOnAxis(
                                    ap=index[a][:, f:f + 1].bitcast(U32), axis=0),
                            ).then_inc(s_rows[a][q], 16)

            pool.iota(row_of[:, :], pattern=[[128, VC]], base=0, channel_multiplier=1).then_inc(s_row_of, 1)
            pool.wait_ge(s_zero, 1)
            pool.affine_select(out=ident[:, :], in_=ident[:, :], compare_op=ALU.not_equal, fill=1.0,
                               base=0, pattern=[[-1, 128]], channel_multiplier=1).then_inc(s_ident, 1)
            pair(0, first=True)
            pair(1)
            with pool.Fori(2, NP) as i:
                pair(i)

        @block.tensor
        def _(pe):
            def turn(i, a, q, first=False):
                n = quads_before(i, a) + q
                quad = quads(first)[q]
                landed = 16 * len(quad)
                if not first:
                    landed = landed * i + (16 * len(quads(True)[q]) if q < NQ0 else 0)
                pe.wait_ge(s_rows[a][q], landed)
                if not (first and a == 0 and q < 2):
                    pe.wait_ge(s_feats, n - 1)
                nq = NQ0 if first else NQ
                for k, f in enumerate(quad):
                    mm = pe.transpose(p_turn[(nq * a + q) % 2][:, k * T:k * T + T], rows[a][:, f, :],
                                      ident[:, :])
                mm.then_inc(s_turned, 1)

            def select(i, k, first=False):
                m = selected(first)
                n = selected_before(i) + k
                t = SEL_FIRST - m + k
                pe.wait_ge(s_onehot, n + 1)
                if first:
                    pe.wait_ge(s_high, 2 * (t + 1))
                    pe.wait_ge(s_low, 2 * (t + 1))
                if not (first and k < 2):
                    pe.wait_ge(s_fsel, n - 1 if (m % 2 == 0 or k >= 2) else n)
                for c in range(VC):
                    r = 128 if c < VC - 1 else VR
                    hot = onehot[k % RING][0:r, c, :]
                    for part in (high, low):
                        mm = pe.matmul(p_sel[k % 2][:, 0:PAIR], part[t][0:r, c, :], hot,
                                       start=(c == 0 and part is high),
                                       stop=(c == VC - 1 and part is low))
                mm.then_inc(s_sel, 1)

            def gram(i, a, banks):
                t = 2 * i + a
                if banks[0] == 0:
                    pe.wait_ge(s_feats, quads_before(i, a + 1) if a == 0 else quads_before(i + 1, 0))
                    pe.wait_ge(s_fsel, selected_before(i + 1))
                    pe.wait_ge(s_fdense, t + 1)
                for b in banks:
                    n = NG * t + b
                    if not (isinstance(n, int) and n < 2):
                        pe.wait_ge(s_prods, n - 1)
                    for k in range(GB):
                        group = feats[a][:, GB * b + k, :, :].rearrange("d j f -> d (j f)")
                        mm = pe.matmul(p_gram[b % 2][0:BLK, BLK * k:BLK * k + BLK], group, group,
                                       start=True, stop=True)
                    mm.then_inc(s_gram, 1)

            def layer1(i, first=False):
                for m in range(M1):
                    if m >= 2:
                        pe.wait_ge(s_h1r, M1 * i + m - 1)
                    elif m == 0 and not first:
                        pe.wait_ge(s_yr, i)
                    cols = slice(128 * m, 128 * m + 128)
                    o = p_mlp[m % 2][:, 0:PAIR]
                    pe.matmul(o, wdense[:, 0, cols], dense[:, bass.ds(i * PAIR, PAIR)], start=True, stop=False)
                    if m == 0:
                        pe.wait_ge(s_pairs, 64 * (i + 1))
                    for c in range(NCH):
                        mm = pe.matmul(o, wpairs[:, c, cols], pairs[:, c, :], start=False,
                                       stop=(c == NCH - 1))
                    mm.then_inc(s_h1, 1)

            def layers23(i):
                pe.wait_ge(s_h1r, M1 * (i + 1))
                for m in range(M2):
                    for k in range(M1):
                        mm = pe.matmul(p_mlp[m % 2][:, 0:PAIR], w2s[:, k, 128 * m:128 * m + 128], h1[:, k, :],
                                       start=(k == 0), stop=(k == M1 - 1))
                    mm.then_inc(s_h2, 1)
                pe.wait_ge(s_h2r, M2 * (i + 1))
                for k in range(M2):
                    mm = pe.matmul(p_mlp[0][0:1, 0:PAIR], w3s[:, k:k + 1], h2[:, k, :], start=(k == 0),
                                   stop=(k == M2 - 1))
                mm.then_inc(s_y, 1)

            def pair(i, first=False, second=False):
                n = selected(first)
                nq = NQ0 if first else NQ
                for q in range(nq):
                    turn(i, 0, q, first)
                    if q < 2 and not first:
                        gram(i - 1, 1, range(4 * q, 4 * q + 4))
                    if q >= 2:
                        for k in range((q - 2) * n // (nq - 2), (q - 1) * n // (nq - 2)):
                            select(i, k, first)
                for q in range(nq):
                    turn(i, 1, q, first)
                    if q < 2:
                        gram(i, 0, range(4 * q, 4 * q + 4))
                    if q == 2 and not first:
                        layer1(i - 1, first=second)
                    if q == 3 and not first:
                        layers23(i - 1)

            pe.wait_ge(s_ident, 1)
            pair(0, first=True)
            pe.wait_ge(s_weights, 96)
            pe.wait_ge(s_wdense, 1)
            pe.wait_ge(s_dense, 16)
            pair(1, second=True)
            with pe.Fori(2, NP) as i:
                pair(i)
            gram(NP - 1, 1, range(NG))
            layer1(NP - 1)
            layers23(NP - 1)

        @block.scalar
        def _(act):
            def keep(i, a, q, first=False):
                quad = quads(first)[q]
                nq = NQ0 if first else NQ
                act.wait_ge(s_turned, quads_before(i, a) + q + 1)
                dst = feats[a][:, :, :, 1 + quad[0]:1 + quad[-1] + 1].rearrange("d g j f -> d f j g")
                src = p_turn[(nq * a + q) % 2][:, 0:len(quad) * T].rearrange("d (f j g) -> d f j g", j=4, g=GS)
                nc.scalar.activation(dst, src, ACT.Copy).then_inc(s_feats, 1)

            def high_bits(k):
                for n, (p, c) in enumerate(PIECES):
                    act.wait_ge(s_masked, 2 * k + n + 1)
                    nc.scalar.activation(high[k][p, c, :], masked[k % STAGES][p, c, :], ACT.Copy)\
                      .then_inc(s_high, 1)

            def keep_dense(i, a):
                src = dense[:, bass.ds((2 * i + a) * T, T)].rearrange("d (j g) -> d j g", j=4)
                nc.scalar.activation(feats[a][:, :, :, 0].rearrange("d g j -> d j g"), src,
                                     ACT.Copy).then_inc(s_fdense, 1)

            def keep_selected(i, k, first=False):
                m = selected(first)
                f = C - m + k
                if k == 0 and not first:
                    act.wait_ge(s_gram, NG * 2 * i)
                act.wait_ge(s_sel, selected_before(i) + k + 1)
                for a in range(2):
                    src = p_sel[k % 2][:, a * T:a * T + T].rearrange("d (j g) -> d j g", j=4)
                    ins = nc.scalar.activation(feats[a][:, :, :, f].rearrange("d g j -> d j g"), src, ACT.Copy)
                ins.then_inc(s_fsel, 1)

            def keep_prods(i, a, banks, first=False):
                t = 2 * i + a
                if banks[0] == 0 and not first:
                    act.wait_ge(s_stored[a], 64 * i)
                for b in banks:
                    act.wait_ge(s_gram, NG * t + b + 1)
                    src = p_gram[b % 2][0:BLK, 0:GB * BLK].rearrange("p (g c) -> p c g", g=GB)
                    nc.scalar.activation(prods[a][0:BLK, :, GB * b:GB * b + GB], src, ACT.Copy)\
                      .then_inc(s_prods, 1)

            def pair(i, first=False, second=False):
                n = selected(first)
                nq = NQ0 if first else NQ
                if not first:
                    act.wait_ge(s_gram, NG * (2 * i - 1))
                keep_dense(i, 0)
                for q in range(nq):
                    keep(i, 0, q, first)
                    if q < 2 and not first:
                        keep_prods(i - 1, 1, range(4 * q, 4 * q + 4), first=second)
                    if q >= 2:
                        for k in range((q - 2) * n // (nq - 2), (q - 1) * n // (nq - 2)):
                            if first and k + 2 < SEL_FIRST:
                                high_bits(k + 2)
                            keep_selected(i, k, first)
                keep_dense(i, 1)
                for q in range(nq):
                    keep(i, 1, q, first)
                    if q < 2:
                        keep_prods(i, 0, range(4 * q, 4 * q + 4), first=first)

            for k in range(2):
                high_bits(k)
            act.wait_ge(s_dense, 16)
            pair(0, first=True)
            pair(1, second=True)
            with act.Fori(2, NP) as i:
                pair(i)
            keep_prods(NP - 1, 1, range(NG))

        @block.vector
        def _(dve):
            def split(k):
                dve.wait_ge(s_table[k], 32)
                if k >= STAGES:
                    dve.wait_ge(s_high, 2 * (k - STAGES + 1))
                old, bits = raw[k % STAGES], masked[k % STAGES]
                for p, c in PIECES:
                    nc.vector.tensor_scalar(bits[p, c, :].bitcast(I32), old[p, c, :].bitcast(I32),
                                            HIGH, None, ALU.bitwise_and).then_inc(s_masked, 1)
                dve.wait_ge(s_masked, 2 * (k + 1))
                for p, c in PIECES:
                    nc.vector.tensor_tensor(low[k][p, c, :], old[p, c, :], bits[p, c, :],
                                            ALU.subtract).then_inc(s_low, 1)

            def make_onehot(i, k, first=False):
                m = selected(first)
                if k == 0:
                    dve.wait_ge(s_ids_all, 16 * (i + 1))
                if k >= RING:
                    dve.wait_ge(s_sel, selected_before(i) + k - RING + 1)
                elif k == 0 and not first:
                    dve.wait_ge(s_sel, selected_before(i))
                at = ids_all[:, SEL_FIRST - m + k, :]
                at = bass.AP(at.tensor, at.offset, [list(at.ap[0]), [0, VC], [1, PAIR]])
                of = row_of[:, :]
                of = bass.AP(of.tensor, of.offset, [list(of.ap[0]), [1, VC], [0, PAIR]])
                nc.vector.tensor_tensor(onehot[k % RING][:, :, :], at, of, ALU.is_equal).then_inc(s_onehot, 1)

            def mlp(i, second=False):
                for m in range(M1):
                    dve.wait_ge(s_h1, M1 * i + m + 1)
                    nc.vector.tensor_scalar(h1[:, m, :], p_mlp[m % 2][:, 0:PAIR], b1s[:, m:m + 1], 0.0,
                                            ALU.add, ALU.max).then_inc(s_h1r, 1)
                for m in range(M2):
                    dve.wait_ge(s_h2, M2 * i + m + 1)
                    nc.vector.tensor_scalar(h2[:, m, :], p_mlp[m % 2][:, 0:PAIR], b2s[:, m:m + 1], 0.0,
                                            ALU.add, ALU.max).then_inc(s_h2r, 1)
                dve.wait_ge(s_y, i + 1)
                if not second:
                    dve.wait_ge(s_out, 16 * i)
                nc.vector.tensor_copy(y[:, :], p_mlp[0][0:1, 0:PAIR]).then_inc(s_yr, 1)

            nc.vector.memset(ident[:, :], 0.0).then_inc(s_zero, 1)
            dve.wait_ge(s_row_of, 1)
            for k in range(SEL_FIRST):
                split(k)
                make_onehot(0, k, first=True)
            dve.wait_ge(s_weights, 96)
            nc.vector.tensor_tensor(wdense[:, 0, :], wdense[:, 0, :], wdense[:, 1, :], ALU.add)\
                     .then_inc(s_wdense, 1)

            def pair(i, second=False):
                for k in range(SEL):
                    make_onehot(i, k)
                mlp(i - 1, second)

            pair(1, second=True)
            with dve.Fori(2, NP) as i:
                pair(i)
            mlp(NP - 1)


def kernel(**inputs):
    import numpy as np
    import concourse.bacc as bacc
    from concourse.bass_utils import run_bass_kernel_spmd

    w1 = np.asarray(inputs["W_top1"])
    order = feature_order([inputs[f"tbl_{n}"].shape[0] for n in range(F)])
    place = [0] + [1 + n for n in order]
    f, g = np.triu_indices(C, k=1)
    row_of = {(int(p), int(q)): D + n for n, (p, q) in enumerate(zip(f, g))}
    rows = [row_of[tuple(sorted(place[p] for p in divmod(r, C)))] for r in pair_rows()]
    ids = np.asarray(inputs["ids"])[:, order]
    arrays = {
        "in_x_t": np.ascontiguousarray(np.asarray(inputs["r_dense_features"]).T),
        "in_ids": np.ascontiguousarray(ids),
        "in_ids_t": np.ascontiguousarray(ids.T),
        "in_w_dense": np.ascontiguousarray(np.stack([w1[0:D], w1[D + len(f):]])),
        "in_w_pairs": np.ascontiguousarray(w1[rows].reshape(NCH, KP, N1)),
        "in_b1": np.ascontiguousarray(np.asarray(inputs["b_top1"]).reshape(M1, 128).T),
        "in_w2": np.ascontiguousarray(inputs["W_top2"]),
        "in_b2": np.ascontiguousarray(np.asarray(inputs["b_top2"]).reshape(M2, 128).T),
        "in_w3": np.ascontiguousarray(np.asarray(inputs["W_top3"]).reshape(M2, 128).T),
    }
    for n in range(F):
        arrays[f"in_table_{n}"] = np.ascontiguousarray(inputs[f"tbl_{order[n]}"])
    nc = bacc.Bacc("TRN2", target_bir_lowering=False, num_devices=1)
    ap = {k: nc.dram_tensor(k, a.shape, mybir.dt.from_np(a.dtype), kind="ExternalInput").ap()
          for k, a in arrays.items()}
    out = nc.dram_tensor("out_y", (B, 1), F32, kind="ExternalOutput").ap()
    program(nc, ap["in_x_t"], ap["in_ids"], ap["in_ids_t"], [ap[f"in_table_{n}"] for n in range(F)],
            ap["in_w_dense"], ap["in_w_pairs"], ap["in_b1"], ap["in_w2"], ap["in_b2"], ap["in_w3"],
            out.rearrange("s a -> a s"))
    r = run_bass_kernel_spmd(nc, [arrays], core_ids=[0])
    return r.results[0]["out_y"]
```

```python
from contextlib import ExitStack

import concourse.bass as bass
from concourse import mybir

F32 = mybir.dt.float32
I32 = mybir.dt.int32
U32 = mybir.dt.uint32
F32R = mybir.dt.float32r
ALU = mybir.AluOpType
ACT = mybir.ActivationFunctionType

B, D, F = 2048, 128, 26
C = F + 1
T = 128
PAIR = 2 * T
NP = B // PAIR
N1, N2 = 512, 256
QUAD = 4
GS = T // 4
BLK = 4 * C
BLKC = 4 * F
GB = 4
NG = GS // GB
HALF = C // 2
RPC = 9
KP = RPC * HALF
NCH = C * HALF // KP
M1, M2 = N1 // 128, N2 // 128

SEL = 7
VS = 1000
VC = -(-VS // 128)
VR = VS - 128 * (VC - 1)
STAGES = BLKC * GS // (VC * D)
RING = 3
EARLY = 2
NGATHER = F - SEL
QUADS = [range(k, min(k + QUAD, NGATHER)) for k in range(0, NGATHER, QUAD)]
NQ = len(QUADS)
HIGH = -(1 << 12)


def feature_order(sizes):
    last = [n for n in range(F) if sizes[n] == VS][-SEL:]
    return [n for n in range(F) if n not in last] + last


def pair_rows():
    rows = [C * p + k for p in range(C - 1) for k in range(HALF)]
    return rows + list(range(HALF, 2 * HALF))


PIECES = ((slice(0, 128), slice(0, VC - 1)), (slice(0, VR), slice(VC - 1, VC)))


def selections(q, first, second):
    n, early = NQ, 0 if first else EARLY if second else 1
    if not (first or second):
        q, n = q - 1, n - 1
        if q < 0:
            return range(0)
    return range(early + q * (SEL - early) // n, early + (q + 1) * (SEL - early) // n)


def program(nc, x_t, ids, ids_t, tables, w_dense, w_pairs, b1, w2, b2, w3, out):
    ctx = ExitStack()
    with ctx:
        def sb(name, shape, dt=F32):
            return ctx.enter_context(nc.sbuf_tensor(name, shape, dt))

        def ps(name):
            return ctx.enter_context(nc.psum_tensor(name, [128, 512], F32))

        def sem(name):
            return ctx.enter_context(nc.semaphore(name))

        square = nc.dram_tensor("square", (C * F, PAIR), F32, kind="Internal").ap()

        ident = sb("ident", [128, 128])
        index = [sb(f"index{a}", [T, F], I32) for a in range(2)]
        rows = [sb(f"rows{a}", [T, NGATHER, D]) for a in range(2)]
        feats = [sb(f"feats{a}", [D, GS, 4, C]) for a in range(2)]
        prods = [sb(f"prods{a}", [128, BLKC, GS]) for a in range(2)]
        piece = [prods[n].rearrange("p c g -> p (c g)")[:, k * VC * D:(k + 1) * VC * D]
                 .rearrange("p (c d) -> p c d", c=VC) for n in range(2) for k in range(STAGES)]
        masked = piece[-1]
        pairs = sb("pairs", [KP, NCH, PAIR])
        ids_all = sb("ids_all", [128, SEL, PAIR], I32)
        row_of = sb("row_of", [128, VC], I32)
        onehot = [sb(f"onehot{k}", [128, VC, PAIR], F32R) for k in range(RING)]
        high = [sb(f"high{k}", [128, VC, D], F32R) for k in range(SEL)]
        low = [sb(f"low{k}", [128, VC, D], F32R) for k in range(SEL)]
        dense = sb("dense", [D, B])
        h1 = sb("h1", [128, M1, PAIR])
        h2 = sb("h2", [128, M2, PAIR])
        wdense = sb("wdense", [D, 2, N1])
        wpairs = sb("wpairs", [KP, NCH, N1])
        w2s = sb("w2s", [128, M1, N2])
        w3s = sb("w3s", [128, M2])
        b1s = sb("b1s", [128, M1])
        b2s = sb("b2s", [128, M2])
        y = sb("y", [T, B // T])

        p_turn = [ps(f"p_turn{k}") for k in range(2)]
        p_gram = [ps(f"p_gram{k}") for k in range(2)]
        p_sel = [ps(f"p_sel{k}") for k in range(2)]
        p_mlp = [ps(f"p_mlp{k}") for k in range(2)]

        def bank1(m, tail):
            return (p_turn + p_sel)[m] if tail else p_mlp[m % 2]

        def bank2(m, tail):
            return p_gram[m] if tail else p_mlp[m]

        s_zero = sem("s_zero")
        s_ident = sem("s_ident")
        s_row_of = sem("s_row_of")
        s_dense = sem("s_dense")
        s_weights = sem("s_weights")
        s_wdense = sem("s_wdense")
        s_table = [sem(f"s_table{k}") for k in range(SEL)]
        s_masked = sem("s_masked")
        s_high = sem("s_high")
        s_low = sem("s_low")
        s_index = [sem(f"s_index{a}") for a in range(2)]
        s_rows = [[sem(f"s_rows{a}_{q}") for q in range(NQ)] for a in range(2)]
        s_turned = sem("s_turned")
        s_feats = sem("s_feats")
        s_fdense = sem("s_fdense")
        s_ids_all = sem("s_ids_all")
        s_onehot = sem("s_onehot")
        s_sel = sem("s_sel")
        s_fsel = sem("s_fsel")
        s_gram = sem("s_gram")
        s_prods = sem("s_prods")
        s_stored = [sem(f"s_stored{a}") for a in range(2)]
        s_pairs = sem("s_pairs")
        s_last = [sem(f"s_last{c}") for c in range(NCH)]
        s_h1 = sem("s_h1")
        s_h1r = sem("s_h1r")
        s_h2 = sem("s_h2")
        s_h2r = sem("s_h2r")
        s_y = sem("s_y")
        s_yr = sem("s_yr")
        s_out = sem("s_out")
        s_passed = sem("s_passed")

        block = ctx.enter_context(nc.Block())

        @block.sync
        def _(sp):
            def load_index(i, a):
                sp.dma_start(index[a][:, :], ids[bass.ds((2 * i + a) * T, T), :]).then_inc(s_index[a], 16)

            def load_ids_all(i):
                src = ids_t[:, bass.ds(i * PAIR, PAIR)]
                src = src.rearrange("(o k) s -> o k s", o=1).to_broadcast([128, SEL, PAIR])
                sp.dma_start(ids_all[:, :, :], src).then_inc(s_ids_all, 16)

            def load_weights():
                sp.dma_start(wdense[:, :, :], w_dense.rearrange("a d n -> d a n")).then_inc(s_weights, 16)
                sp.dma_start(wpairs[:, :, :], w_pairs.rearrange("c p n -> p c n")).then_inc(s_weights, 16)
                sp.dma_start(w2s[:, :, :], w2.rearrange("(k p) n -> p k n", p=128)).then_inc(s_weights, 16)
                sp.dma_start(w3s[:, :], w3).then_inc(s_weights, 16)
                sp.dma_start(b1s[:, :], b1).then_inc(s_weights, 16)
                sp.dma_start(b2s[:, :], b2).then_inc(s_weights, 16)

            for a in range(2):
                load_index(0, a)
            for k in range(SEL):
                t = tables[F - 1 - k]
                whole = 128 * (VC - 1)
                raw = piece[k % STAGES]
                if k >= STAGES:
                    sp.wait_ge(s_low, 2 * (k - STAGES + 1))
                sp.dma_start(raw[:, 0:VC - 1, :], t[0:whole, :].rearrange("(c p) d -> p c d", p=128))\
                  .then_inc(s_table[k], 16)
                sp.dma_start(raw[0:VR, VC - 1, :], t[whole:VS, :]).then_inc(s_table[k], 16)
                if k == 0:
                    load_ids_all(0)
                if k == 1:
                    sp.dma_start(dense[:, 0:PAIR], x_t[:, 0:PAIR]).then_inc(s_dense, 16)

            def store(i, a, first=False):
                sp.wait_ge(s_prods, (2 * i + a + 1) * NG)
                sp.sem_inc(s_passed, 1)
                if a == 0 and not first:
                    sp.wait_ge(s_pairs, 64 * i)
                for j in range(4):
                    dst = square.rearrange("(f g) s -> f g s", g=F)
                    lo = a * T + j * GS
                    sp.dma_start(dst[:, :, lo:lo + GS], prods[a][C * j:C * j + C, F * j:F * j + F, :])\
                      .then_inc(s_stored[a], 16)

            def read_back(i, tiles, first=False):
                for a in tiles:
                    sp.wait_ge(s_stored[a], 64 * i + 64)
                    sp.sem_inc(s_passed, 1)
                if not first:
                    sp.wait_ge(s_h1, M1 * i)
                at, n = tiles[0] * T, len(tiles) * T
                for c in range(NCH):
                    done = s_last[c] if tiles == (1,) else s_pairs
                    k = min(RPC, C - 1 - c * RPC)
                    src = bass.AP(square.tensor, C * RPC * c * PAIR + at,
                                  [[C * PAIR, k], [PAIR, HALF], [1, n]])
                    sp.dma_start(pairs[0:k * HALF, c, at:at + n], src).then_inc(done, 16)
                src = bass.AP(square.tensor, HALF * PAIR + at, [[PAIR, HALF], [1, n]])
                sp.dma_start(pairs[KP - HALF:KP, NCH - 1, at:at + n], src).then_inc(done, 16)

            def pair(i, first=False, second=False, last=False):
                if not first:
                    store(i - 1, 1, first=second)
                    read_back(i - 1, (0, 1), first=second)
                if not last:
                    sp.wait_ge(s_onehot, SEL * (i + 1))
                    sp.sem_inc(s_passed, 1)
                    load_ids_all(i + 1)
                    sp.wait_ge(s_turned, NQ * (2 * i + 1))
                    sp.sem_inc(s_passed, 1)
                    load_index(i + 1, 0)
                if first:
                    sp.dma_start(dense[:, PAIR:B], x_t[:, PAIR:B]).then_inc(s_dense, 16)
                store(i, 0, first=first)
                if not last:
                    sp.wait_ge(s_turned, NQ * (2 * i + 2))
                    sp.sem_inc(s_passed, 1)
                    load_index(i + 1, 1)
                if first:
                    load_weights()
                if last:
                    read_back(i, (0,))

            pair(0, first=True)
            pair(1, second=True)
            with sp.Fori(2, NP - 1) as i:
                pair(i)
            pair(NP - 1, last=True)
            store(NP - 1, 1)
            read_back(NP - 1, (1,))
            sp.wait_ge(s_yr, NP + 1)
            sp.dma_start(out, y[:, :]).then_inc(s_out, 16)
            sp.wait_ge(s_out, 16)

        @block.gpsimd
        def _(pool):
            def pair(i, first=False):
                for a in range(2):
                    pool.wait_ge(s_index[a], 16 * (i + 1))
                    pool.sem_inc(s_passed, 1)
                    for q, quad in enumerate(QUADS):
                        if not first:
                            pool.wait_ge(s_turned, NQ * (2 * i - 2 + a) + q + 1)
                            pool.sem_inc(s_passed, 1)
                        for f in quad:
                            pool.indirect_dma_start(
                                out=rows[a][:, f, :], out_offset=None, in_=tables[f],
                                in_offset=bass.IndirectOffsetOnAxis(
                                    ap=index[a][:, f:f + 1].bitcast(U32), axis=0),
                            ).then_inc(s_rows[a][q], 16)

            pool.iota(row_of[:, :], pattern=[[128, VC]], base=0, channel_multiplier=1).then_inc(s_row_of, 1)
            pool.wait_ge(s_zero, 1)
            pool.affine_select(out=ident[:, :], in_=ident[:, :], compare_op=ALU.not_equal, fill=1.0,
                               base=0, pattern=[[-1, 128]], channel_multiplier=1).then_inc(s_ident, 1)
            pair(0, first=True)
            pair(1)
            with pool.Fori(2, NP) as i:
                pair(i)

        @block.tensor
        def _(pe):
            def turn(i, a, q, first=False):
                n = NQ * (2 * i + a) + q
                quad = QUADS[q]
                pe.wait_ge(s_rows[a][q], 16 * len(quad) * (i + 1))
                if not (first and a == 0 and q < 2):
                    pe.wait_ge(s_feats, n - 1)
                for k, f in enumerate(quad):
                    mm = pe.transpose(p_turn[(NQ * a + q) % 2][:, k * T:k * T + T], rows[a][:, f, :],
                                      ident[:, :])
                mm.then_inc(s_turned, 1)

            def select(i, k, first=False, second=False):
                n = SEL * i + k
                pe.wait_ge(s_onehot, n + 1)
                if first or second:
                    pe.wait_ge(s_high, 2 * (k + 1))
                    pe.wait_ge(s_low, 2 * (k + 1))
                if not (first and k < 2):
                    pe.wait_ge(s_fsel, n - 1 if SEL % 2 == 0 or k > 0 else n)
                for c in range(VC):
                    r = 128 if c < VC - 1 else VR
                    hot = onehot[k % RING][0:r, c, :]
                    for part in (high, low):
                        mm = pe.matmul(p_sel[k % 2][:, 0:PAIR], part[k][0:r, c, :], hot,
                                       start=(c == 0 and part is high),
                                       stop=(c == VC - 1 and part is low))
                mm.then_inc(s_sel, 1)

            def gram(i, a, banks):
                t = 2 * i + a
                if banks[0] == 0:
                    pe.wait_ge(s_feats, NQ * (t + 1))
                    pe.wait_ge(s_fsel, SEL * (i + 1))
                    pe.wait_ge(s_fdense, t + 1)
                for b in banks:
                    n = NG * t + b
                    if not (isinstance(n, int) and n < 2):
                        pe.wait_ge(s_prods, n - 1)
                    for k in range(GB):
                        group = feats[a][:, GB * b + k, :, :].rearrange("d j f -> d (j f)")
                        mm = pe.matmul(p_gram[b % 2][0:BLK, BLKC * k:BLKC * k + BLKC], group,
                                       feats[a][:, GB * b + k, :, 1:C], start=True, stop=True)
                    mm.then_inc(s_gram, 1)

            def layer1(i, m, first=False):
                if m >= 2:
                    pe.wait_ge(s_h1r, M1 * i + m - 1)
                elif m == 0 and not first:
                    pe.wait_ge(s_yr, i)
                cols = slice(128 * m, 128 * m + 128)
                pe.matmul(bank1(m, False)[:, 0:PAIR], wdense[:, 0, cols], dense[:, bass.ds(i * PAIR, PAIR)],
                          start=True, stop=False)
                if m == 0:
                    pe.wait_ge(s_pairs, 64 * (i + 1))
                for c in range(NCH):
                    mm = pe.matmul(bank1(m, False)[:, 0:PAIR], wpairs[:, c, cols], pairs[:, c, :],
                                   start=False, stop=(c == NCH - 1))
                mm.then_inc(s_h1, 1)

            def layer1_dense(tile):
                for m in range(M1):
                    pe.matmul(bank1(m, True)[:, 0:T], wdense[:, 0, 128 * m:128 * m + 128],
                              dense[:, tile * T:tile * T + T], start=True, stop=False)

            def layer1_pairs(own, last=False):
                for c in range(NCH):
                    if last:
                        pe.wait_ge(s_last[c], 32 if c == NCH - 1 else 16)
                    elif c == 0:
                        pe.wait_ge(s_pairs, 64 * NP)
                    for m in range(M1):
                        mm = pe.matmul(bank1(m, True)[:, 0:T], wpairs[:, c, 128 * m:128 * m + 128],
                                       pairs[:, c, own], start=False, stop=(c == NCH - 1))
                        if c == NCH - 1:
                            mm.then_inc(s_h1, 1)

            def layer2(u, own, blocks=range(M2), tail=False):
                if not tail:
                    pe.wait_ge(s_h1r, M1 * (u + 1))
                for m in blocks:
                    for k in range(M1):
                        if tail and m == 0:
                            pe.wait_ge(s_h1r, M1 * u + k + 1)
                        mm = pe.matmul(bank2(m, tail)[:, 0:own.stop - own.start],
                                       w2s[:, k, 128 * m:128 * m + 128], h1[:, k, own],
                                       start=(k == 0), stop=(k == M1 - 1))
                    mm.then_inc(s_h2, 1)

            def layer3(u, own):
                for a in range(own.start // T, own.stop // T):
                    for k in range(M2):
                        if a == own.start // T and (k == 0 or own.stop - own.start == T):
                            pe.wait_ge(s_h2r, M2 * u + (k + 1 if own.stop - own.start == T else M2))
                        mm = pe.matmul(p_mlp[0][:, a:a + 1], h2[:, k, a * T:a * T + T], w3s[:, k:k + 1],
                                       start=(k == 0), stop=(k == M2 - 1))
                mm.then_inc(s_y, 1)

            both = slice(0, PAIR)

            def pair(i, first=False, second=False, last=False):
                if second:
                    gram(0, 1, range(NG))
                for q in range(NQ):
                    turn(i, 0, q, first)
                    if q < 2 and not (first or second):
                        gram(i - 1, 1, range(4 * q, 4 * q + 2))
                        if q == 0:
                            select(i, 0)
                        gram(i - 1, 1, range(4 * q + 2, 4 * q + 4))
                    for k in selections(q, first, second):
                        select(i, k, first, second)
                if second:
                    pe.wait_ge(s_weights, 96)
                    pe.wait_ge(s_wdense, 1)
                    pe.wait_ge(s_dense, 32)
                for q in range(NQ):
                    turn(i, 1, q, first)
                    if q < 2:
                        for b in range(4 * q, 4 * q + 4, 2):
                            if not first:
                                layer1(i - 1, b // 2, first=second)
                            gram(i, 0, (b, b + 1))
                    if first and q < EARLY:
                        select(1, q, second=True)
                    if q == 2 and not (first or last):
                        layer2(i - 1, both)
                    if q == NQ - 1 and not (first or last):
                        layer3(i - 1, both)
                    if q >= NQ - M2 and last:
                        layer2(i - 1, both, (q - NQ + M2,))

            pe.wait_ge(s_ident, 1)
            pair(0, first=True)
            pair(1, second=True)
            with pe.Fori(2, NP - 1) as i:
                pair(i)
            pair(NP - 1, last=True)
            gram(NP - 1, 1, range(NG))
            layer1_dense(2 * (NP - 1))
            layer3(NP - 2, both)
            layer1_pairs(slice(0, T))
            pe.wait_ge(s_prods, 2 * NP * NG)
            layer2(NP - 1, slice(0, T), tail=True)
            layer1_dense(2 * NP - 1)
            pe.wait_ge(s_yr, NP - 1)
            layer3(NP - 1, slice(0, T))
            layer1_pairs(slice(T, PAIR), last=True)
            layer2(NP, slice(T, PAIR), tail=True)
            pe.wait_ge(s_yr, NP)
            layer3(NP, slice(T, PAIR))

        @block.scalar
        def _(act):
            def keep(i, a, q, first=False):
                quad = QUADS[q]
                act.wait_ge(s_turned, NQ * (2 * i + a) + q + 1)
                dst = feats[a][:, :, :, 1 + quad[0]:1 + quad[-1] + 1].rearrange("d g j f -> d f j g")
                src = p_turn[(NQ * a + q) % 2][:, 0:len(quad) * T].rearrange("d (f j g) -> d f j g", j=4, g=GS)
                nc.scalar.activation(dst, src, ACT.Copy).then_inc(s_feats, 1)

            def high_bits(k):
                for m, (p, c) in enumerate(PIECES):
                    act.wait_ge(s_masked, 2 * k + m + 1)
                    nc.scalar.activation(high[k][p, c, :], masked[p, c, :], ACT.Copy).then_inc(s_high, 1)

            def keep_dense(i, a):
                src = dense[:, bass.ds((2 * i + a) * T, T)].rearrange("d (j g) -> d j g", j=4)
                nc.scalar.activation(feats[a][:, :, :, 0].rearrange("d g j -> d j g"), src,
                                     ACT.Copy).then_inc(s_fdense, 1)

            def keep_selected(i, k, first=False):
                f = C - 1 - k
                if k == 0 and not first:
                    act.wait_ge(s_gram, NG * 2 * i)
                act.wait_ge(s_sel, SEL * i + k + 1)
                for a in range(2):
                    src = p_sel[k % 2][:, a * T:a * T + T].rearrange("d (j g) -> d j g", j=4)
                    ins = nc.scalar.activation(feats[a][:, :, :, f].rearrange("d g j -> d j g"), src, ACT.Copy)
                ins.then_inc(s_fsel, 1)

            def keep_prods(i, a, banks, first=False):
                t = 2 * i + a
                if first and a == 1:
                    act.wait_ge(s_low, 2 * SEL)
                if banks[0] == 0 and not first:
                    act.wait_ge(s_stored[a], 64 * i)
                for b in banks:
                    act.wait_ge(s_gram, NG * t + b + 1)
                    src = p_gram[b % 2][0:BLK, 0:GB * BLKC].rearrange("p (g c) -> p c g", g=GB)
                    nc.scalar.activation(prods[a][0:BLK, :, GB * b:GB * b + GB], src, ACT.Copy)\
                      .then_inc(s_prods, 1)

            def pair(i, first=False, second=False):
                if not first:
                    act.wait_ge(s_gram, NG * (2 * i - 1))
                keep_dense(i, 0)
                if second:
                    keep_prods(0, 1, range(NG), first=True)
                for q in range(NQ):
                    keep(i, 0, q, first)
                    if not (first or second) and q < 2:
                        keep_prods(i - 1, 1, range(4 * q, 4 * q + 4))
                    if second and q == 0:
                        for k in range(EARLY):
                            keep_selected(i, k)
                    if q == 1 and not (first or second):
                        keep_selected(i, 0)
                    for k in selections(q, first, second):
                        if first and k + 2 < SEL:
                            high_bits(k + 2)
                        keep_selected(i, k, first)
                keep_dense(i, 1)
                for q in range(NQ):
                    keep(i, 1, q, first)
                    if q < 2:
                        keep_prods(i, 0, range(4 * q, 4 * q + 4), first=first)

            for k in range(2):
                high_bits(k)
            act.wait_ge(s_dense, 16)
            pair(0, first=True)
            act.wait_ge(s_dense, 32)
            pair(1, second=True)
            with act.Fori(2, NP) as i:
                pair(i)
            keep_prods(NP - 1, 1, range(NG))

        @block.vector
        def _(dve):
            def split(k):
                dve.wait_ge(s_table[k], 32)
                if k > 0:
                    dve.wait_ge(s_high, 2 * k)
                    dve.wait_ge(s_low, 2 * k)
                raw = piece[k % STAGES]
                for p, c in PIECES:
                    nc.vector.tensor_scalar(masked[p, c, :].bitcast(I32), raw[p, c, :].bitcast(I32),
                                            HIGH, None, ALU.bitwise_and).then_inc(s_masked, 1)
                dve.wait_ge(s_masked, 2 * (k + 1))
                for p, c in PIECES:
                    nc.vector.tensor_tensor(low[k][p, c, :], raw[p, c, :], masked[p, c, :],
                                            ALU.subtract).then_inc(s_low, 1)

            def make_onehot(i, k, first=False):
                if k == 0:
                    dve.wait_ge(s_ids_all, 16 * (i + 1))
                if k >= RING:
                    dve.wait_ge(s_sel, SEL * i + k - RING + 1)
                elif k == 0 and not first:
                    dve.wait_ge(s_sel, SEL * i)
                at = ids_all[:, k, :]
                at = bass.AP(at.tensor, at.offset, [list(at.ap[0]), [0, VC], [1, PAIR]])
                of = row_of[:, :]
                of = bass.AP(of.tensor, of.offset, [list(of.ap[0]), [1, VC], [0, PAIR]])
                nc.vector.tensor_tensor(onehot[k % RING][:, :, :], at, of, ALU.is_equal).then_inc(s_onehot, 1)

            def relu1(u, own, m, tail=False):
                dve.wait_ge(s_h1, M1 * u + m + 1)
                nc.vector.tensor_scalar(h1[:, m, own], bank1(m, tail)[:, 0:own.stop - own.start],
                                        b1s[:, m:m + 1], 0.0, ALU.add, ALU.max).then_inc(s_h1r, 1)

            def relu2(u, own, m, tail=False):
                dve.wait_ge(s_h2, M2 * u + m + 1)
                nc.vector.tensor_scalar(h2[:, m, own], bank2(m, tail)[:, 0:own.stop - own.start],
                                        b2s[:, m:m + 1], 0.0, ALU.add, ALU.max).then_inc(s_h2r, 1)

            def result(u, tile, own):
                own = slice(own.start // T, own.stop // T)
                dve.wait_ge(s_y, u + 1)
                nc.vector.tensor_copy(y[:, bass.ds(tile, own.stop - own.start)], p_mlp[0][:, own])\
                         .then_inc(s_yr, 1)

            nc.vector.memset(ident[:, :], 0.0).then_inc(s_zero, 1)
            dve.wait_ge(s_row_of, 1)
            for k in range(SEL):
                split(k)
                make_onehot(0, k, first=True)
            def pair(i, second=False, last=False):
                own = slice(0, PAIR)
                for k in range(RING, SEL):
                    make_onehot(i, k)
                if second:
                    dve.wait_ge(s_weights, 96)
                    nc.vector.tensor_tensor(wdense[:, 0, :], wdense[:, 0, :], wdense[:, 1, :], ALU.add)\
                             .then_inc(s_wdense, 1)
                for m in range(M1):
                    relu1(i - 1, own, m)
                    if m % 2 == 1 and not last:
                        make_onehot(i + 1, m // 2)
                for m in range(M2):
                    relu2(i - 1, own, m)
                result(i - 1, 2 * (i - 1), own)
                if not last:
                    for k in range(M1 // 2, RING):
                        make_onehot(i + 1, k)

            for k in range(RING):
                make_onehot(1, k)
            pair(1, second=True)
            with dve.Fori(2, NP - 1) as i:
                pair(i)
            pair(NP - 1, last=True)
            for a in range(2):
                own = slice(a * T, a * T + T)
                for m in range(M1):
                    relu1(NP - 1 + a, own, m, tail=True)
                for m in range(M2):
                    relu2(NP - 1 + a, own, m, tail=True)
                result(NP - 1 + a, 2 * (NP - 1) + a, own)


def kernel(**inputs):
    import numpy as np
    import concourse.bacc as bacc
    from concourse.bass_utils import run_bass_kernel_spmd

    w1 = np.asarray(inputs["W_top1"])
    order = feature_order([inputs[f"tbl_{n}"].shape[0] for n in range(F)])
    place = [0] + [1 + n for n in order]
    f, g = np.triu_indices(C, k=1)
    row_of = {(int(p), int(q)): D + n for n, (p, q) in enumerate(zip(f, g))}
    rows = [row_of[tuple(sorted((place[r // F], place[r % F + 1])))] for r in pair_rows()]
    ids = np.asarray(inputs["ids"])[:, order]
    arrays = {
        "in_x_t": np.ascontiguousarray(np.asarray(inputs["r_dense_features"]).T),
        "in_ids": np.ascontiguousarray(ids),
        "in_ids_t": np.ascontiguousarray(ids.T[:F - 1 - SEL:-1]),
        "in_w_dense": np.ascontiguousarray(np.stack([w1[0:D], w1[D + len(f):]])),
        "in_w_pairs": np.ascontiguousarray(w1[rows].reshape(NCH, KP, N1)),
        "in_b1": np.ascontiguousarray(np.asarray(inputs["b_top1"]).reshape(M1, 128).T),
        "in_w2": np.ascontiguousarray(inputs["W_top2"]),
        "in_b2": np.ascontiguousarray(np.asarray(inputs["b_top2"]).reshape(M2, 128).T),
        "in_w3": np.ascontiguousarray(np.asarray(inputs["W_top3"]).reshape(M2, 128).T),
    }
    for n in range(F):
        arrays[f"in_table_{n}"] = np.ascontiguousarray(inputs[f"tbl_{order[n]}"])
    nc = bacc.Bacc("TRN2", target_bir_lowering=False, num_devices=1)
    ap = {k: nc.dram_tensor(k, a.shape, mybir.dt.from_np(a.dtype), kind="ExternalInput").ap()
          for k, a in arrays.items()}
    out = nc.dram_tensor("out_y", (T, B // T), F32, kind="ExternalOutput").ap()
    program(nc, ap["in_x_t"], ap["in_ids"], ap["in_ids_t"], [ap[f"in_table_{n}"] for n in range(F)],
            ap["in_w_dense"], ap["in_w_pairs"], ap["in_b1"], ap["in_w2"], ap["in_b2"], ap["in_w3"],
            out)
    r = run_bass_kernel_spmd(nc, [arrays], core_ids=[0])
    return np.ascontiguousarray(r.results[0]["out_y"].T).reshape(B, 1)
```
